# Optimizing a Trainium2 kernel written in Bass

```python
import numpy as np
import jax
import jax.numpy as jnp

def _softmax(x, axis=-1):
    return jax.nn.softmax(x, axis=axis)

def _gelu(x):
    return jax.nn.gelu(x, approximate=True)

def _silu(x):
    return jax.nn.silu(x)

def _sigmoid(x):
    return jax.nn.sigmoid(x)

def _layernorm(x, axis=-1, eps=1e-05):
    m = jnp.mean(x, axis=axis, keepdims=True)
    v = jnp.var(x, axis=axis, keepdims=True)
    return (x - m) / jnp.sqrt(v + eps)

def _scatter_add(tgt, idx, src, axis=0):
    return tgt.at[idx].add(src)

def _segment_sum(src, seg, n):
    return jax.ops.segment_sum(src, seg, n)
kernel_name = 'mk_cond_resid_d1_seqx_r4_9cdeb0'

def setup_inputs(seed: int=0):
    np.random.seed(seed)
    _w = jnp.asarray

    def _rec_inputs():
        import jax
        import jax.numpy as jnp
        _rk = jax.random.key(seed)
        x = -0.0003929 + 0.9999 * jax.random.normal(jax.random.fold_in(_rk, 1), (64, 64, 256), jnp.float32)
        _lenS = 64 - jax.random.randint(jax.random.fold_in(_rk, 7), (64,), 0, max(1, 64 // 4) + 1, jnp.int32)
        _lenS2 = 64 - jax.random.randint(jax.random.fold_in(_rk, 8), (64,), 0, max(1, 64 // 4) + 1, jnp.int32)
        itok_B_0_63 = jax.random.randint(jax.random.fold_in(_rk, 11), (64,), 0, 64, jnp.int32)
        return (x, itok_B_0_63)
    x, itok_B_0_63 = _rec_inputs()

    def _L0_cond_setup():
        import jax, jax.numpy as jnp
        import numpy as np
        NUM_CATEGORIES = 64
        INPUT_DIM = 256
        HIDDEN_DIM = 256
        B = 64
        S = 64
        key = jax.random.key(seed)
        kx, kc, kw = jax.random.split(key, 3)
        x = jax.random.normal(kx, (B, S, INPUT_DIM), dtype=jnp.float32)
        cat_ids = jax.random.randint(kc, (B,), 0, NUM_CATEGORIES, dtype=jnp.int32)
        W = 0.02 * jax.random.normal(kw, (NUM_CATEGORIES, INPUT_DIM, HIDDEN_DIM), dtype=jnp.float32)
        b = jnp.zeros((NUM_CATEGORIES, HIDDEN_DIM), dtype=jnp.float32)
        return {'x': x, 'cat_ids': cat_ids, 'W': W, 'b': b}
    _L0_cond_all = _L0_cond_setup()
    _L0_cond_in = {k: v for k, v in _L0_cond_all.items() if k in ('W', 'b')}
    del _L0_cond_all
    return {'x': x, 'itok_B_0_63': itok_B_0_63, 'L0_cond_W': _L0_cond_in['W'], 'L0_cond_b': _L0_cond_in['b']}

def reference(x, itok_B_0_63, L0_cond_W, L0_cond_b):
    import jax
    import jax.numpy as jnp

    def _L0_cond_ref(x, cat_ids, W, b):
        import jax, jax.numpy as jnp
        import numpy as np
        NUM_CATEGORIES = 64
        INPUT_DIM = 256
        HIDDEN_DIM = 256
        B = 64
        S = 64
        selected_W = W[cat_ids]
        selected_b = b[cat_ids]
        out = jnp.einsum('bsd,bdh->bsh', x, selected_W) + selected_b[:, None, :]
        return out
    x = x + _L0_cond_ref(x, itok_B_0_63, L0_cond_W, L0_cond_b)
    return x

_drawn_inputs = setup_inputs


def setup_inputs(seed=0):
    import zlib

    import numpy as np

    out = dict(_drawn_inputs(seed))
    spreads = {'L0_cond_b': (0.0, 0.1)}
    factors = {}
    for name, (base, spread) in spreads.items():
        noise = np.random.default_rng([zlib.crc32(name.encode()), seed]).standard_normal(out[name].shape)
        drawn = base * np.exp(spread * noise) if base else spread * noise
        out[name] = jnp.asarray(drawn.astype(out[name].dtype))
    for name, factor in factors.items():
        out[name] = (out[name] * factor).astype(out[name].dtype)
    return out
```

```python
import concourse.bass as bass
from concourse import mybir
from contextlib import ExitStack


def conditional_residual(nc, x, cat_ids, w, bias, out):
    f32, bf16, i32 = mybir.dt.float32, mybir.dt.bfloat16, mybir.dt.int32
    ALU = mybir.AluOpType
    ACT = mybir.ActivationFunctionType

    P = 128
    B, S, D = x.shape
    C, _, H = w.shape
    E = D // P
    PAIR = P // S
    TILES = 2
    G = PAIR * TILES
    GROUPS = B // G
    RING = 4
    PASSES = GROUPS // RING
    PARTS = 3
    BAND = 32
    BANDS = B // BAND
    SLOTS = 2

    x_dram = x.rearrange("(g t b) s d -> g (b s) t d", t=TILES, b=PAIR)
    out_dram = out.rearrange("(g t b) s d -> g (b s) t d", t=TILES, b=PAIR)
    w_dram = w.rearrange("c (p e) h -> c p (e h)", e=E)
    ids_dram = cat_ids.rearrange("(o b) -> o b", o=1)

    with ExitStack() as ctx:
        def sb(name, shape, dt):
            return ctx.enter_context(nc.sbuf_tensor(name, shape, dt))

        def ps(name, shape, dt):
            return ctx.enter_context(nc.psum_tensor(name, shape, dt))

        def sem(name):
            return ctx.enter_context(nc.semaphore(name))

        w_sb = sb("w_sb", [P, C * E * H], f32)
        x_sb = sb("x_sb", [P, RING, TILES, D], f32)
        xt_sb = sb("xt_sb", [P, RING, TILES, E, P], f32)
        out_sb = sb("out_sb", [P, RING, TILES, H], f32)
        base_sb = sb("base_sb", [P, RING, TILES, H], f32)
        ids_all = sb("ids_all", [P, B], i32)
        ids_col = sb("ids_col", [B, 1], i32)
        first_row = sb("first_row", [1, B], i32)
        earlier = sb("earlier", [B, B], f32)
        repeats = sb("repeats", [B, B], bf16)
        ones_col = sb("ones_col", [B, 1], bf16)
        category = sb("category", [C, 1], f32)
        ident = sb("ident", [P, P], f32)
        table = sb("table", [C, H], f32)
        has_category = sb("has_category", [C, BANDS, PARTS, BAND], f32)
        rest = sb("rest", [PARTS * BAND, BANDS, H], f32)
        low = sb("low", [PARTS * BAND, BANDS, H], f32)
        mid = sb("mid", [PARTS * BAND, BANDS, H], bf16)
        bias_parts = sb("bias_parts", [PARTS * BAND, BANDS, H], bf16)
        own_rows = sb("own_rows", [PARTS * BAND, BAND, S], bf16)

        xt_ps = [ps(f"xt_ps{n}", [P, TILES, E, P], f32) for n in range(SLOTS)]
        bias_ps = [ps(f"bias_ps{n}", [P, TILES, H], f32) for n in range(SLOTS)]
        out_ps = [[ps(f"out_ps{n}_{b}", [S, TILES, H], f32) for b in range(PAIR)] for n in range(SLOTS)]

        ids_loaded = sem("ids_loaded")
        ids_col_loaded = sem("ids_col_loaded")
        table_loaded = sem("table_loaded")
        earlier_step = sem("earlier_step")
        ident_step = sem("ident_step")
        own_step = sem("own_step")
        category_made = sem("category_made")
        repeats_made = sem("repeats_made")
        counted = sem("counted")
        first_made = sem("first_made")
        has_category_made = sem("has_category_made")
        bias_gathered = sem("bias_gathered")
        split_step = sem("split_step")
        bias_split = sem("bias_split")
        x_loaded = [sem(f"x_loaded{k}") for k in range(RING)]
        w_loaded = [sem(f"w_loaded{n}") for n in range(RING * G)]
        transposed = sem("transposed")
        xt_ready = sem("xt_ready")
        bias_spread = sem("bias_spread")
        based = sem("based")
        multiplied = sem("multiplied")
        added = sem("added")
        stored = [sem(f"stored{k}") for k in range(RING)]

        block = ctx.enter_context(nc.Block())

        def passes(eng, body):
            body(0, first=True, last=False)
            with eng.Fori(1, PASSES - 1) as i:
                body(i, first=False, last=False)
            body(PASSES - 1, first=False, last=True)

        def values(eng, row, start, n, top):
            return nc.values_load_multi_w_load_instructions(
                row[0:1, bass.ds(start, n)], engines=[eng.engine], min_val=0, max_val=top,
                skip_runtime_bounds_check_because="category numbers are below C by the reference's contract")[1]

        @block.sync
        def _(sp):
            sp.dma_start(ids_all[:, :], ids_dram.to_broadcast([P, B])).then_inc(ids_loaded, 16)
            sp.dma_start(ids_col[:, :], cat_ids.rearrange("(b o) -> b o", o=1)).then_inc(ids_col_loaded, 16)

            def load_w(n, cat, cond):
                sp.dma_start(w_sb[:, bass.ds(cat * (E * H), E * H)], w_dram[bass.ds(cat, 1)].rearrange("c p f -> (c p) f"),
                             **cond).then_inc(w_loaded[n], 16)

            def load_ws(k, start, reuse):
                cats = values(sp, ids_all, start, G, C - 1)
                firsts = values(sp, first_row, start, G, 1)
                for n in range(G):
                    slot = k * G + n
                    if reuse is not None:
                        sp.wait_ge(w_loaded[slot], 16 * reuse)
                    load_w(slot, cats[n], {"cond": firsts[n]})

            sp.wait_ge(ids_loaded, 16)
            cat0 = values(sp, ids_all, 0, 1, C - 1)[0]
            load_w(0, cat0, {})
            for k in range(1, RING):
                sp.dma_start(x_sb[:, k], x_dram[k]).then_inc(x_loaded[k], 16)
            sp.wait_ge(first_made, 1)
            cats = values(sp, ids_all, 1, G - 1, C - 1)
            firsts = values(sp, first_row, 1, G - 1, 1)
            for n in range(1, G):
                load_w(n, cats[n - 1], {"cond": firsts[n - 1]})
            for k in range(1, RING):
                load_ws(k, k * G, None)

            def body(i, first, last):
                if last:
                    return
                for k in range(RING):
                    load_ws(k, (i + 1) * (RING * G) + k * G, i + 1)
                    sp.wait_ge(added, PAIR * (i * RING + k + 1))
                    sp.dma_start(x_sb[:, k], x_dram[bass.ds((i + 1) * RING + k, 1)].rearrange("g p t d -> (g p) t d")).then_inc(x_loaded[k], 16)

            passes(sp, body)

        @block.scalar
        def _(act):
            act.dma_start(x_sb[:, 0], x_dram[0]).then_inc(x_loaded[0], 16)
            act.dma_start(table[:, :], bias).then_inc(table_loaded, 16)

            def copy_xt(i, k, first):
                act.wait_ge(transposed, i * RING + k + 1)
                if not first:
                    act.wait_ge(multiplied, (i - 1) * RING + k + 1)
                nc.scalar.activation(xt_sb[:, k], xt_ps[k % SLOTS][:], ACT.Copy).then_inc(xt_ready, 1)

            copy_xt(0, 0, True)

            def body(i, first, last):
                for k in range(RING):
                    if k < RING - 1:
                        copy_xt(i, k + 1, first)
                    elif not last:
                        copy_xt(i + 1, 0, False)
                    act.wait_ge(added, PAIR * (i * RING + k + 1))
                    act.dma_start(out_dram[bass.ds(i * RING + k, 1)].rearrange("g p t d -> (g p) t d"), out_sb[:, k]).then_inc(stored[k], 16)

            passes(act, body)
            for k in range(RING):
                act.wait_ge(stored[k], 16 * PASSES)

        @block.gpsimd
        def _(pool):
            nc.gpsimd.memset(earlier[:], 1.0).then_inc(earlier_step, 1)
            nc.gpsimd.memset(ident[:], 0.0).then_inc(ident_step, 1)
            nc.gpsimd.iota(category[:], pattern=[[0, 1]], base=0, channel_multiplier=1,
                           allow_small_or_imprecise_dtypes=True).then_inc(category_made, 1)
            nc.gpsimd.memset(own_rows[:], 0.0).then_inc(own_step, 1)
            pool.wait_ge(earlier_step, 1)
            nc.gpsimd.affine_select(out=earlier[:], in_=earlier[:], compare_op=ALU.is_gt, fill=0.0, base=0,
                                    pattern=[[1, B]], channel_multiplier=-1).then_inc(earlier_step, 1)
            pool.wait_ge(ident_step, 1)
            nc.gpsimd.affine_select(out=ident[:], in_=ident[:], compare_op=ALU.not_equal, fill=1.0, base=0,
                                    pattern=[[-1, P]], channel_multiplier=1).then_inc(ident_step, 1)
            pool.wait_ge(ident_step, 2)
            for part in range(PARTS):
                pool.wait_ge(own_step, part + 1)
                rows = own_rows[part * BAND:(part + 1) * BAND]
                nc.gpsimd.affine_select(out=rows, in_=rows, compare_op=ALU.not_equal, fill=1.0, base=0,
                                        pattern=[[-1, BAND], [0, S]], channel_multiplier=1).then_inc(own_step, 1)

        @block.vector
        def _(dve):
            nc.vector.memset(ones_col[:], 1.0)
            dve.wait_ge(earlier_step, 2)
            dve.wait_ge(ids_loaded, 16)
            dve.wait_ge(ids_col_loaded, 16)
            nc.vector.scalar_tensor_tensor(out=repeats[:], in0=ids_all[0:B, :], scalar=ids_col[:, 0:1], in1=earlier[:],
                                           op0=ALU.is_equal, op1=ALU.mult).then_inc(repeats_made, 1)
            dve.wait_ge(category_made, 1)
            for part in range(PARTS):
                last = nc.vector.tensor_scalar(has_category[:, :, part, :], ids_all[0:C, :].rearrange("c (n b) -> c n b", b=BAND),
                                               category[:, 0:1], None, ALU.is_equal)
            last.then_inc(has_category_made, 1)
            dve.wait_ge(counted, 1)
            nc.vector.tensor_scalar(first_row[:], out_ps[1][0][0:1, 0, 0:B], 0.0, None, ALU.is_equal).then_inc(first_made, 1)

            dve.wait_ge(bias_gathered, 1)
            nc.vector.tensor_copy(bias_parts[:], bias_ps[1][0:PARTS * BAND]).then_inc(split_step, 1)
            dve.wait_ge(split_step, 1)
            nc.vector.tensor_tensor(rest[:], bias_ps[1][0:PARTS * BAND], bias_parts[:], ALU.subtract).then_inc(split_step, 1)
            dve.wait_ge(split_step, 2)
            nc.vector.tensor_copy(mid[:], rest[:]).then_inc(split_step, 1)
            dve.wait_ge(split_step, 3)
            nc.vector.tensor_tensor(low[:], rest[:], mid[:], ALU.subtract).then_inc(split_step, 1)
            nc.vector.tensor_copy(bias_parts[BAND:2 * BAND], mid[BAND:2 * BAND])
            dve.wait_ge(split_step, 4)
            nc.vector.tensor_copy(bias_parts[2 * BAND:3 * BAND], low[2 * BAND:3 * BAND]).then_inc(bias_split, 1)

            def add_base(i, k, first):
                dve.wait_ge(bias_spread, i * RING + k + 1)
                nc.vector.tensor_tensor(base_sb[:, k], bias_ps[k % SLOTS][:], x_sb[:, k], ALU.add).then_inc(based, 1)

            add_base(0, 0, True)

            def body(i, first, last):
                for k in range(RING):
                    if k < RING - 1:
                        add_base(i, k + 1, first)
                    elif not last:
                        add_base(i + 1, 0, False)
                    dve.wait_ge(multiplied, i * RING + k + 1)
                    dve.wait_ge(based, i * RING + k + 1)
                    if not first:
                        dve.wait_ge(stored[k], 16 * i)
                    for b in range(PAIR):
                        rows = slice(b * S, (b + 1) * S)
                        nc.vector.tensor_tensor(out_sb[rows, k], out_ps[k % SLOTS][b][:], base_sb[rows, k], ALU.add).then_inc(added, 1)

            passes(dve, body)

        @block.tensor
        def _(pe):
            def prepare(i, k, first):
                g = i * RING + k
                early = first and k < SLOTS
                pe.wait_ge(x_loaded[k], 16 * (i + 1))
                if not early:
                    pe.wait_ge(xt_ready, g - SLOTS + 1)
                for t in range(TILES):
                    for e in range(E):
                        last = nc.tensor.transpose(xt_ps[k % SLOTS][:, t, e, :], x_sb[:, k, t, e::E], ident[:])
                last.then_inc(transposed, 1)
                if not early:
                    pe.wait_ge(based, g - SLOTS + 1)
                for t in range(TILES):
                    tile = g * TILES + t
                    band, at = tile // (BAND // PAIR), tile % (BAND // PAIR)
                    last = nc.tensor.matmul(bias_ps[k % SLOTS][:, t, :], own_rows[:, bass.ds(at * PAIR, PAIR), :],
                                            bias_parts[:, band, :], start=True, stop=True)
                last.then_inc(bias_spread, 1)

            def products(i, k, first):
                g = i * RING + k
                cats = values(pe, ids_all, g * G, G, C - 1)
                if not (first and k < SLOTS):
                    pe.wait_ge(added, PAIR * (g - SLOTS + 1))
                pe.wait_ge(xt_ready, g + 1)
                for t in range(TILES):
                    for b in range(PAIR):
                        n = t * PAIR + b
                        pe.wait_ge(w_loaded[k * G + n], 16 * (i + 1))
                        for e in range(E):
                            last = nc.tensor.matmul(out_ps[k % SLOTS][b][:, t, :], xt_sb[:, k, t, e, b * S:(b + 1) * S],
                                                    w_sb[:, bass.ds(cats[n] * (E * H) + e * H, H)],
                                                    start=(e == 0), stop=(e == E - 1))
                last.then_inc(multiplied, 1)

            pe.wait_ge(repeats_made, 1)
            nc.tensor.matmul(out_ps[1][0][0:1, 0, 0:B], ones_col[:], repeats[:], start=True, stop=True).then_inc(counted, 1)
            pe.wait_ge(has_category_made, 1)
            pe.wait_ge(table_loaded, 16)
            for n in range(BANDS):
                last = nc.tensor.matmul(bias_ps[1][0:PARTS * BAND, n, :], has_category[:, n].rearrange("c p b -> c (p b)"), table[:],
                                        start=True, stop=True)
            last.then_inc(bias_gathered, 1)
            pe.wait_ge(ident_step, 2)
            pe.wait_ge(own_step, 1 + PARTS)
            pe.wait_ge(bias_split, 1)
            pe.wait_ge(ids_loaded, 16)
            prepare(0, 0, True)

            def body(i, first, last):
                for k in range(RING):
                    if k < RING - 1:
                        prepare(i, k + 1, first)
                    elif not last:
                        prepare(i + 1, 0, False)
                    products(i, k, first)

            passes(pe, body)


_INS = ["x", "itok_B_0_63", "L0_cond_W", "L0_cond_b"]


def kernel(**inputs):
    import numpy as np
    import concourse.bacc as bacc
    from concourse import mybir as mb
    from concourse.bass_utils import run_bass_kernel_spmd

    nc = bacc.Bacc("TRN2", target_bir_lowering=False, num_devices=1)
    arrays, args = {}, []
    for name in _INS:
        a = np.ascontiguousarray(inputs[name])
        arrays[f"in_{name}"] = a
        args.append(nc.dram_tensor(f"in_{name}", a.shape, mb.dt.from_np(a.dtype), kind="ExternalInput").ap())
    shape, dtype = inputs["x"].shape, np.dtype("float32")
    out = nc.dram_tensor("out", shape, mb.dt.from_np(dtype), kind="ExternalOutput").ap()
    conditional_residual(nc, *args, out)
    return run_bass_kernel_spmd(nc, [arrays], core_ids=[0]).results[0]["out"]
```

```python
import concourse.bass as bass
from concourse import mybir
from contextlib import ExitStack


def conditional_residual(nc, x, cat_ids, w, bias, out):
    f32, bf16, i32 = mybir.dt.float32, mybir.dt.bfloat16, mybir.dt.int32
    ALU = mybir.AluOpType
    ACT = mybir.ActivationFunctionType

    P = 128
    B, S, D = x.shape
    C, _, H = w.shape
    E = D // P
    PAIR = P // S
    TILES = 2
    G = PAIR * TILES
    GROUPS = B // G
    RING = 4
    PASSES = GROUPS // RING
    SLOTS = 2
    PARTS = 3
    BAND = 32
    BANDS = B // BAND

    x_dram = x.rearrange("(g t b) s d -> g (b s) t d", t=TILES, b=PAIR)
    out_dram = out.rearrange("(g t b) s d -> g (b s) t d", t=TILES, b=PAIR)
    w_dram = w.rearrange("c (p e) h -> c p (e h)", e=E)

    with ExitStack() as ctx:
        def sb(name, shape, dt):
            return ctx.enter_context(nc.sbuf_tensor(name, shape, dt))

        def ps(name, shape, dt):
            return ctx.enter_context(nc.psum_tensor(name, shape, dt))

        def sem(name):
            return ctx.enter_context(nc.semaphore(name))

        w_sb = sb("w_sb", [P, C * E * H], f32)
        w_ring = sb("w_ring", [P, SLOTS, G, E, H], f32)
        x_sb = sb("x_sb", [P, RING, TILES, D], f32)
        xt_sb = sb("xt_sb", [P, RING, TILES, E, P], f32)
        out_sb = sb("out_sb", [P, RING, TILES, H], f32)
        ids_all = sb("ids_all", [C, B], i32)
        ids_col = sb("ids_col", [B, 1], i32)
        first_row = sb("first_row", [1, B], i32)
        after = sb("after", [B, B], f32)
        earlier = sb("earlier", [B, B], f32)
        repeats = sb("repeats", [B, B], bf16)
        ones_col = sb("ones_col", [B, 1], bf16)
        category = sb("category", [C, 1], f32)
        off_diagonal = sb("off_diagonal", [P, P], f32)
        ident = sb("ident", [P, P], f32)
        table = sb("table", [C, H], f32)
        has_category = sb("has_category", [C, BANDS, PARTS, BAND], f32)
        rest = sb("rest", [PARTS * BAND, BANDS, H], f32)
        low = sb("low", [PARTS * BAND, BANDS, H], f32)
        mid = sb("mid", [PARTS * BAND, BANDS, H], bf16)
        bias_parts = sb("bias_parts", [PARTS * BAND, BANDS, H], bf16)
        off_band = sb("off_band", [PARTS * BAND, BAND], f32)
        own_rows = sb("own_rows", [PARTS * BAND, BAND, S], bf16)

        xt_ps = [ps(f"xt_ps{n}", [P, TILES, E, P], f32) for n in range(SLOTS)]
        out_ps = [ps(f"out_ps{n}", [P, TILES, H], f32) for n in range(RING)]
        count_ps = ps("count_ps", [1, 512], f32)
        gather_ps = ps("gather_ps", [PARTS * BAND, BANDS, H], f32)

        ids_loaded = sem("ids_loaded")
        ids_col_loaded = sem("ids_col_loaded")
        table_loaded = sem("table_loaded")
        after_made = sem("after_made")
        off_diagonal_made = sem("off_diagonal_made")
        off_band_made = sem("off_band_made")
        category_made = sem("category_made")
        earlier_made = sem("earlier_made")
        ident_made = sem("ident_made")
        own_rows_made = sem("own_rows_made")
        repeats_made = sem("repeats_made")
        counted = sem("counted")
        first_made = sem("first_made")
        has_category_made = sem("has_category_made")
        bias_gathered = sem("bias_gathered")
        split_step = sem("split_step")
        bias_split = sem("bias_split")
        x_loaded = [sem(f"x_loaded{k}") for k in range(RING)]
        w_loaded = [sem(f"w_loaded{n}") for n in range(RING * G)]
        w_copied = [sem("w_copied_by_act"), sem("w_copied_by_dve")]
        transposed = sem("transposed")
        xt_ready = sem("xt_ready")
        multiplied = sem("multiplied")
        added = sem("added")
        stored = [sem(f"stored{k}") for k in range(RING)]

        block = ctx.enter_context(nc.Block())

        def passes(eng, ahead, finish):
            def one(i, first, last):
                for k in range(RING):
                    if k < RING - 1:
                        ahead(i, k + 1, first)
                    elif not last:
                        ahead(i + 1, 0, False)
                    finish(i, k, first)

            ahead(0, 0, True)
            one(0, True, False)
            with eng.Fori(1, PASSES - 1) as i:
                one(i, False, False)
            one(PASSES - 1, False, True)

        def values(eng, row, start, n, top):
            return nc.values_load_multi_w_load_instructions(
                row[0:1, bass.ds(start, n)], engines=[eng.engine], min_val=0, max_val=top,
                skip_runtime_bounds_check_because="category numbers are below C by the reference's contract")[1]

        def slot(cat):
            return w_sb[:, bass.ds(cat * (E * H), E * H)]

        def copy_weights(eng, copy, mine, i, k, first):
            cats = values(eng, ids_all, (i * RING + k) * G, G, C - 1)
            if not (first and k < SLOTS):
                eng.wait_ge(multiplied, i * RING + k - SLOTS + 1)
            for n in range(G):
                eng.wait_ge(w_loaded[k * G + n], 16 * (i + 1))
                if n % 2 == mine:
                    copy(w_ring[:, k % SLOTS, n].rearrange("p e h -> p (e h)"), slot(cats[n])).then_inc(w_copied[mine], 1)

        @block.sync
        def _(sp):
            sp.dma_start(ids_all[:, :], cat_ids.rearrange("(o b) -> o b", o=1).to_broadcast([C, B])).then_inc(ids_loaded, 16)
            sp.dma_start(ids_col[:, :], cat_ids.rearrange("(b o) -> b o", o=1)).then_inc(ids_col_loaded, 16)
            for k in range(1, RING):
                sp.dma_start(x_sb[:, k], x_dram[k]).then_inc(x_loaded[k], 16)

            def load_weights(k, n, cat, **cond):
                sp.dma_start(slot(cat), w_dram[bass.ds(cat, 1)].rearrange("c p f -> (c p) f"), **cond).then_inc(w_loaded[k * G + n], 16)

            sp.wait_ge(ids_loaded, 16)
            load_weights(0, 0, values(sp, ids_all, 0, 1, C - 1)[0])
            sp.wait_ge(first_made, 1)
            for k in range(RING):
                cats = values(sp, ids_all, k * G, G, C - 1)
                firsts = values(sp, first_row, k * G, G, 1)
                for n in range(G):
                    if (k, n) != (0, 0):
                        load_weights(k, n, cats[n], cond=firsts[n])

            def load_next_pass(i, k):
                cats = values(sp, ids_all, ((i + 1) * RING + k) * G, G, C - 1)
                firsts = values(sp, first_row, ((i + 1) * RING + k) * G, G, 1)
                for n in range(G):
                    sp.wait_ge(w_loaded[k * G + n], 16 * (i + 1))
                    load_weights(k, n, cats[n], cond=firsts[n])
                sp.wait_ge(added, i * RING + k + 1)
                sp.dma_start(x_sb[:, k], x_dram[bass.ds((i + 1) * RING + k, 1)].rearrange("g p t d -> (g p) t d")).then_inc(x_loaded[k], 16)

            with sp.Fori(0, PASSES - 1) as i:
                for k in range(RING):
                    load_next_pass(i, k)

        @block.scalar
        def _(act):
            act.dma_start(x_sb[:, 0], x_dram[0]).then_inc(x_loaded[0], 16)
            act.dma_start(table[:, :], bias).then_inc(table_loaded, 16)

            def copy(dst, src):
                return nc.scalar.activation(dst, src, ACT.Copy)

            def ahead(i, k, first):
                act.wait_ge(transposed, i * RING + k + 1)
                if not first:
                    act.wait_ge(multiplied, (i - 1) * RING + k + 1)
                copy(xt_sb[:, k], xt_ps[k % SLOTS][:]).then_inc(xt_ready, 1)
                if first and k == 0:
                    act.wait_ge(ids_loaded, 16)
                copy_weights(act, copy, 0, i, k, first)

            def finish(i, k, first):
                act.wait_ge(added, i * RING + k + 1)
                act.dma_start(out_dram[bass.ds(i * RING + k, 1)].rearrange("g p t d -> (g p) t d"), out_sb[:, k]).then_inc(stored[k], 16)

            passes(act, ahead, finish)
            for k in range(RING):
                act.wait_ge(stored[k], 16 * PASSES)

        @block.gpsimd
        def _(pool):
            def count(out, columns, step, multiplier):
                return nc.gpsimd.iota(out, pattern=[[step, columns]], base=0, channel_multiplier=multiplier,
                                      allow_small_or_imprecise_dtypes=True)

            count(off_diagonal[:], P, -1, 1).then_inc(off_diagonal_made, 1)
            count(after[:], B, 1, -1).then_inc(after_made, 1)
            count(category[:], 1, 0, 1).then_inc(category_made, 1)
            for part in range(PARTS):
                if part == 0:
                    pool.wait_ge(category_made, 1)
                else:
                    pool.wait_ge(off_band_made, part)
                count(off_band[part * BAND:(part + 1) * BAND, :], BAND, -1, 1).then_inc(off_band_made, 1)

        @block.vector
        def _(dve):
            nc.vector.memset(ones_col[:], 1.0)
            dve.wait_ge(off_diagonal_made, 1)
            nc.vector.tensor_scalar(ident[:], off_diagonal[:], 0.0, None, ALU.is_equal).then_inc(ident_made, 1)
            dve.wait_ge(after_made, 1)
            nc.vector.tensor_scalar(earlier[:], after[:], 0.0, None, ALU.is_gt).then_inc(earlier_made, 1)
            dve.wait_ge(earlier_made, 1)
            dve.wait_ge(ids_loaded, 16)
            dve.wait_ge(ids_col_loaded, 16)
            nc.vector.scalar_tensor_tensor(out=repeats[:], in0=ids_all[0:B, :], scalar=ids_col[:, 0:1], in1=earlier[:],
                                           op0=ALU.is_equal, op1=ALU.mult).then_inc(repeats_made, 1)
            dve.wait_ge(category_made, 1)
            for part in range(PARTS):
                last = nc.vector.tensor_scalar(has_category[:, :, part, :], ids_all[0:C, :].rearrange("c (n b) -> c n b", b=BAND),
                                               category[:, 0:1], None, ALU.is_equal)
            last.then_inc(has_category_made, 1)
            dve.wait_ge(counted, 1)
            nc.vector.tensor_scalar(first_row[:], count_ps[0:1, 0:B], 0.0, None, ALU.is_equal).then_inc(first_made, 1)
            dve.wait_ge(off_band_made, PARTS)
            nc.vector.tensor_scalar(own_rows[:], off_band[:].unsqueeze(2).to_broadcast([PARTS * BAND, BAND, S]),
                                    0.0, None, ALU.is_equal).then_inc(own_rows_made, 1)

            dve.wait_ge(bias_gathered, 1)
            nc.vector.tensor_copy(bias_parts[:], gather_ps[:]).then_inc(split_step, 1)
            dve.wait_ge(split_step, 1)
            nc.vector.tensor_tensor(rest[:], gather_ps[:], bias_parts[:], ALU.subtract).then_inc(split_step, 1)
            dve.wait_ge(split_step, 2)
            nc.vector.tensor_copy(mid[:], rest[:]).then_inc(split_step, 1)
            dve.wait_ge(split_step, 3)
            nc.vector.tensor_tensor(low[:], rest[:], mid[:], ALU.subtract).then_inc(split_step, 1)
            nc.vector.tensor_copy(bias_parts[BAND:2 * BAND], mid[BAND:2 * BAND])
            dve.wait_ge(split_step, 4)
            nc.vector.tensor_copy(bias_parts[2 * BAND:3 * BAND], low[2 * BAND:3 * BAND]).then_inc(bias_split, 1)

            def ahead(i, k, first):
                copy_weights(dve, nc.vector.tensor_copy, 1, i, k, first)

            def finish(i, k, first):
                dve.wait_ge(multiplied, i * RING + k + 1)
                if not first:
                    dve.wait_ge(stored[k], 16 * i)
                nc.vector.tensor_tensor(out_sb[:, k], out_ps[k][:], x_sb[:, k], ALU.add).then_inc(added, 1)

            passes(dve, ahead, finish)

        @block.tensor
        def _(pe):
            def ahead(i, k, first):
                g = i * RING + k
                pe.wait_ge(x_loaded[k], 16 * (i + 1))
                if not (first and k < SLOTS):
                    pe.wait_ge(xt_ready, g - SLOTS + 1)
                for t in range(TILES):
                    for e in range(E):
                        last = nc.tensor.transpose(xt_ps[k % SLOTS][:, t, e, :], x_sb[:, k, t, e::E], ident[:])
                last.then_inc(transposed, 1)
                if first and k == 0:
                    pe.wait_ge(own_rows_made, 1)
                    pe.wait_ge(bias_split, 1)
                if not first:
                    pe.wait_ge(added, (i - 1) * RING + k + 1)
                for t in range(TILES):
                    tile = g * TILES + t
                    band, at = tile // (BAND // PAIR), tile % (BAND // PAIR)
                    nc.tensor.matmul(out_ps[k][:, t, :], own_rows[:, bass.ds(at * PAIR, PAIR), :], bias_parts[:, band, :],
                                     start=(t == 0), stop=False, skip_group_check=True)

            def finish(i, k, first):
                g = i * RING + k
                pe.wait_ge(xt_ready, g + 1)
                for t in range(TILES):
                    for half in range(2):
                        pe.wait_ge(w_copied[half], g * TILES + t + 1)
                    for e in range(E):
                        for b in range(PAIR):
                            last = nc.tensor.matmul(out_ps[k][b * S:(b + 1) * S, t, :], xt_sb[:, k, t, e, b * S:(b + 1) * S],
                                                    w_ring[:, k % SLOTS, t * PAIR + b, e, :],
                                                    start=False, stop=(e == E - 1), skip_group_check=True)
                last.then_inc(multiplied, 1)

            pe.wait_ge(repeats_made, 1)
            nc.tensor.matmul(count_ps[0:1, 0:B], ones_col[:], repeats[:], start=True, stop=True).then_inc(counted, 1)
            pe.wait_ge(has_category_made, 1)
            pe.wait_ge(table_loaded, 16)
            for n in range(BANDS):
                last = nc.tensor.matmul(gather_ps[:, n, :], has_category[:, n].rearrange("c p b -> c (p b)"), table[:],
                                        start=(n == 0), stop=True, skip_group_check=True)
            last.then_inc(bias_gathered, 1)
            pe.wait_ge(ident_made, 1)

            passes(pe, ahead, finish)


_INS = ["x", "itok_B_0_63", "L0_cond_W", "L0_cond_b"]


def kernel(**inputs):
    import numpy as np
    import concourse.bacc as bacc
    from concourse import mybir as mb
    from concourse.bass_utils import run_bass_kernel_spmd

    nc = bacc.Bacc("TRN2", target_bir_lowering=False, num_devices=1)
    arrays, args = {}, []
    for name in _INS:
        a = np.ascontiguousarray(inputs[name])
        arrays[f"in_{name}"] = a
        args.append(nc.dram_tensor(f"in_{name}", a.shape, mb.dt.from_np(a.dtype), kind="ExternalInput").ap())
    shape, dtype = inputs["x"].shape, np.dtype("float32")
    out = nc.dram_tensor("out", shape, mb.dt.from_np(dtype), kind="ExternalOutput").ap()
    conditional_residual(nc, *args, out)
    return run_bass_kernel_spmd(nc, [arrays], core_ids=[0]).results[0]["out"]
```

```python
import concourse.bass as bass
from concourse import mybir
from contextlib import ExitStack


def conditional_residual(nc, x, cat_ids, w, bias, out):
    f32, bf16, i32 = mybir.dt.float32, mybir.dt.bfloat16, mybir.dt.int32
    ALU = mybir.AluOpType
    ACT = mybir.ActivationFunctionType

    P = 128
    B, S, D = x.shape
    C, _, H = w.shape
    E = D // P
    PAIR = P // S
    TILES = 2
    G = PAIR * TILES
    GROUPS = B // G
    RING = 4
    PASSES = GROUPS // RING
    SLOTS = 2
    IN_FLIGHT = 9
    OUTS = 3 * RING
    EARLY = (GROUPS - OUTS) // (PASSES - 2)
    PARTS = 3
    BAND = 32
    BANDS = B // BAND

    x_dram = x.rearrange("(g t b) s d -> g (b s) t d", t=TILES, b=PAIR)
    out_dram = out.rearrange("(n b) s d -> (b s) n d", b=PAIR)
    w_dram = w.rearrange("c (p e) h -> c p (e h)", e=E)

    with ExitStack() as ctx:
        def sb(name, shape, dt):
            return ctx.enter_context(nc.sbuf_tensor(name, shape, dt))

        def ps(name, shape, dt):
            return ctx.enter_context(nc.psum_tensor(name, shape, dt))

        def sem(name):
            return ctx.enter_context(nc.semaphore(name))

        w_sb = sb("w_sb", [P, C * E * H], f32)
        w_ring = sb("w_ring", [P, RING, G, E, H], f32)
        x_sb = sb("x_sb", [P, RING, TILES, D], f32)
        xt_sb = sb("xt_sb", [P, SLOTS, TILES, E, P], f32)
        out_sb = sb("out_sb", [P, OUTS * TILES * H], f32)
        ids_all = sb("ids_all", [C, B], i32)
        ids_col = sb("ids_col", [B, 1], i32)
        first_row = sb("first_row", [1, B], i32)
        after = sb("after", [B, B], f32)
        earlier = sb("earlier", [B, B], f32)
        repeats = sb("repeats", [B, B], bf16)
        ones_col = sb("ones_col", [B, 1], bf16)
        category = sb("category", [C, 1], f32)
        off_diagonal = sb("off_diagonal", [P, P], f32)
        ident = sb("ident", [P, P], f32)
        table = sb("table", [C, H], f32)
        has_category = sb("has_category", [C, BANDS, PARTS, BAND], f32)
        rest = out_sb[0:PARTS * BAND, -2 * BANDS * H:-BANDS * H].rearrange("p (n h) -> p n h", n=BANDS)
        low = out_sb[0:PARTS * BAND, -BANDS * H:].rearrange("p (n h) -> p n h", n=BANDS)
        mid = sb("mid", [PARTS * BAND, BANDS, H], bf16)
        bias_parts = sb("bias_parts", [PARTS * BAND, BANDS, H], bf16)
        off_band = sb("off_band", [PARTS * BAND, BAND], f32)
        own_rows = sb("own_rows", [PARTS * BAND, BAND, S], bf16)

        xt_ps = [ps(f"xt_ps{n}", [P, TILES, E, P], f32) for n in range(SLOTS)]
        out_ps = [ps(f"out_ps{n}", [P, TILES, H], f32) for n in range(RING)]
        side_ps = [ps(f"side_ps{n}", [P, 512], f32) for n in range(BANDS)]
        count_ps = side_ps[1][0:1, 0:B]
        gather_ps = [bank[0:PARTS * BAND, 0:H] for bank in side_ps]

        ids_loaded = sem("ids_loaded")
        ids_col_loaded = sem("ids_col_loaded")
        table_loaded = sem("table_loaded")
        after_made = sem("after_made")
        off_diagonal_made = sem("off_diagonal_made")
        off_band_made = sem("off_band_made")
        category_made = sem("category_made")
        earlier_made = sem("earlier_made")
        ident_made = sem("ident_made")
        own_rows_made = sem("own_rows_made")
        repeats_made = sem("repeats_made")
        counted = sem("counted")
        first_made = sem("first_made")
        has_category_made = sem("has_category_made")
        bias_gathered = sem("bias_gathered")
        split_step = sem("split_step")
        bias_split = sem("bias_split")
        x_loaded = [sem(f"x_loaded{k}") for k in range(RING)]
        w_loaded = [sem(f"w_loaded{n}") for n in range(RING * G)]
        w_copied = [sem("w_copied_by_act"), sem("w_copied_by_dve")]
        transposed = sem("transposed")
        xt_ready = sem("xt_ready")
        multiplied = sem("multiplied")
        added = sem("added")
        early_stored = sem("early_stored")
        late_stored = sem("late_stored")

        block = ctx.enter_context(nc.Block())

        def passes(eng, *stages):
            def one(i, is_first, is_last):
                for k in range(RING):
                    for ahead, do in stages:
                        over, at = divmod(k + ahead, RING)
                        if not (is_last and over):
                            do(i + over, at, is_first and not over, is_last)

            for ahead, do in stages:
                for k in range(ahead):
                    do(0, k, True, False)
            one(0, True, False)
            with eng.Fori(1, PASSES - 1) as i:
                one(i, False, False)
            one(PASSES - 1, False, True)

        def values(eng, row, start, n, top):
            return nc.values_load_multi_w_load_instructions(
                row[0:1, bass.ds(start, n)], engines=[eng.engine], min_val=0, max_val=top,
                skip_runtime_bounds_check_because="category numbers are below C by the reference's contract")[1]

        def result(i, k):
            return results(i * RING + k, TILES)

        def results(m, n):
            return out_sb[:, bass.ds((m % (OUTS * TILES // n)) * (n * H), n * H)].rearrange("p (t h) -> p t h", h=H)

        def store(eng, m, n, done):
            eng.dma_start(out_dram[:, bass.ds(m * n, n), :], results(m, n)).then_inc(done, 16)

        def last_ps(t):
            return out_ps[RING - 1][:, t, :] if t < TILES - 1 else side_ps[0][:, 0:H]

        def slot(cat):
            return w_sb[:, bass.ds(cat * (E * H), E * H)]

        def copy_weights(eng, copy, mine, i, k, first):
            if first and k == 0:
                eng.wait_ge(ids_loaded, 16)
            cats = values(eng, ids_all, (i * RING + k) * G, G, C - 1)
            if not first:
                eng.wait_ge(multiplied, (i - 1) * RING + k + 1)
            for n in range(G):
                eng.wait_ge(w_loaded[k * G + n], 16 * (i + 1))
                if n % 2 == mine:
                    copy(w_ring[:, k, n].rearrange("p e h -> p (e h)"), slot(cats[n])).then_inc(w_copied[mine], 1)

        @block.sync
        def _(sp):
            ids_dram = cat_ids.rearrange("(o b) -> o b", o=1)
            sp.dma_start(ids_all[:, :], ids_dram.to_broadcast([C, B])).then_inc(ids_loaded, 16)

            def load_weights(i, n, cat, **cond):
                over, at = divmod(n - IN_FLIGHT, RING * G)
                if over == 0:
                    sp.wait_ge(w_loaded[at], 16 * (i + 1))
                elif not isinstance(i, int):
                    sp.wait_ge(w_loaded[at], 16 * i)
                sp.dma_start(slot(cat), w_dram[bass.ds(cat, 1)].rearrange("c p f -> (c p) f"), **cond).then_inc(w_loaded[n], 16)

            cats = values(sp, ids_dram, 0, G, C - 1)
            load_weights(0, 0, cats[0])
            for n in range(1, G):
                is_new = cats[n] != cats[0]
                for m in range(1, n):
                    is_new = is_new * (cats[n] != cats[m])
                load_weights(0, n, cats[n], cond=is_new)

            sp.wait_ge(ids_loaded, 16)
            cats = values(sp, ids_all, 0, RING * G, C - 1)
            sp.wait_ge(first_made, 1)
            firsts = values(sp, first_row, 0, RING * G, 1)
            for n in range(G, RING * G):
                load_weights(0, n, cats[n], cond=firsts[n])

            with sp.Fori(1, PASSES) as i:
                cats = values(sp, ids_all, i * (RING * G), RING * G, C - 1)
                firsts = values(sp, first_row, i * (RING * G), RING * G, 1)
                for n in range(RING * G):
                    load_weights(i, n, cats[n], cond=firsts[n])

            with sp.Fori((GROUPS - OUTS) // 2, GROUPS // 2 - 1) as m:
                sp.wait_ge(added, m * 2 + 2)
                store(sp, m, 2 * TILES, late_stored)
            sp.wait_ge(added, GROUPS - 1)
            store(sp, GROUPS - 2, TILES, late_stored)
            for t in range(TILES):
                sp.wait_ge(added, GROUPS + t)
                store(sp, (GROUPS - 1) * TILES + t, 1, late_stored)
            sp.wait_ge(late_stored, 16 * (OUTS // 2 - 1 + 1 + TILES))

        @block.scalar
        def _(act):
            act.dma_start(x_sb[:, 0], x_dram[0]).then_inc(x_loaded[0], 16)
            act.dma_start(x_sb[:, 1], x_dram[1]).then_inc(x_loaded[1], 16)

            def copy(dst, src):
                return nc.scalar.activation(dst, src, ACT.Copy)

            def copy_transposes(i, k, first, last):
                act.wait_ge(transposed, i * RING + k + 1)
                if not (first and k < SLOTS):
                    act.wait_ge(multiplied, i * RING + k - SLOTS + 1)
                copy(xt_sb[:, k % SLOTS], xt_ps[k % SLOTS][:]).then_inc(xt_ready, 1)

            def copy_own(i, k, first, last):
                if first and k + 2 < RING:
                    act.dma_start(x_sb[:, k + 2], x_dram[k + 2]).then_inc(x_loaded[k + 2], 16)
                copy_weights(act, copy, 0, i, k, first)

            def transfers(i, k, first, last):
                g = i * RING + k
                if not (first and k == 0) and not (last and k > 0):
                    act.wait_ge(added, g)
                    at = (k + RING - 1) % RING
                    act.dma_start(x_sb[:, at], x_dram[bass.ds(g + RING - 1, 1)].rearrange("g p t d -> (g p) t d")).then_inc(x_loaded[at], 16)
                if not first and not last and (k + 1) % (RING // EARLY) == 0:
                    store(act, (i - 1) * EARLY + k // (RING // EARLY), TILES, early_stored)

            passes(act, (1, copy_transposes), (0, transfers), (2, copy_own))
            act.wait_ge(early_stored, 16 * (GROUPS - OUTS))

        @block.gpsimd
        def _(pool):
            def count(out, columns, step, multiplier):
                return nc.gpsimd.iota(out, pattern=[[step, columns]], base=0, channel_multiplier=multiplier,
                                      allow_small_or_imprecise_dtypes=True)

            count(off_diagonal[:], P, -1, 1).then_inc(off_diagonal_made, 1)
            count(after[:], B, 1, -1).then_inc(after_made, 1)
            pool.dma_start(ids_col[:, :], cat_ids.rearrange("(b o) -> b o", o=1)).then_inc(ids_col_loaded, 16)
            count(category[:], 1, 0, 1).then_inc(category_made, 1)
            for part in range(PARTS):
                if part == 0:
                    pool.wait_ge(category_made, 1)
                else:
                    pool.wait_ge(off_band_made, part)
                count(off_band[part * BAND:(part + 1) * BAND, :], BAND, -1, 1).then_inc(off_band_made, 1)
            pool.dma_start(table[:, :], bias).then_inc(table_loaded, 16)

        @block.vector
        def _(dve):
            nc.vector.memset(ones_col[:], 1.0)
            dve.wait_ge(off_diagonal_made, 1)
            nc.vector.tensor_scalar(ident[:], off_diagonal[:], 0.0, None, ALU.is_equal).then_inc(ident_made, 1)
            dve.wait_ge(after_made, 1)
            nc.vector.tensor_scalar(earlier[:], after[:], 0.0, None, ALU.is_gt).then_inc(earlier_made, 1)
            dve.wait_ge(off_band_made, PARTS)
            nc.vector.tensor_scalar(own_rows[:], off_band[:].unsqueeze(2).to_broadcast([PARTS * BAND, BAND, S]),
                                    0.0, None, ALU.is_equal).then_inc(own_rows_made, 1)
            dve.wait_ge(earlier_made, 1)
            dve.wait_ge(ids_loaded, 16)
            dve.wait_ge(ids_col_loaded, 16)
            nc.vector.scalar_tensor_tensor(out=repeats[:], in0=ids_all[0:B, :], scalar=ids_col[:, 0:1], in1=earlier[:],
                                           op0=ALU.is_equal, op1=ALU.mult).then_inc(repeats_made, 1)
            dve.wait_ge(category_made, 1)

            def mark_categories(n):
                ids = ids_all[:, n * BAND:(n + 1) * BAND].unsqueeze(1).to_broadcast([C, PARTS, BAND])
                nc.vector.tensor_scalar(has_category[:, n], ids, category[:, 0:1], None, ALU.is_equal).then_inc(has_category_made, 1)

            mark_categories(0)
            dve.wait_ge(counted, 1)
            nc.vector.tensor_scalar(first_row[:], count_ps, 0.0, None, ALU.is_equal).then_inc(first_made, 1)
            for n in range(1, BANDS):
                mark_categories(n)

            def split_bias(n):
                step = 4 * n
                parts = bias_parts[:, n]
                dve.wait_ge(bias_gathered, n + 1)
                nc.vector.tensor_copy(parts, gather_ps[n]).then_inc(split_step, 1)
                dve.wait_ge(split_step, step + 1)
                nc.vector.tensor_tensor(rest[:, n], gather_ps[n], parts, ALU.subtract).then_inc(split_step, 1)
                dve.wait_ge(split_step, step + 2)
                nc.vector.tensor_copy(mid[:, n], rest[:, n]).then_inc(split_step, 1)
                dve.wait_ge(split_step, step + 3)
                nc.vector.tensor_tensor(low[:, n], rest[:, n], mid[:, n], ALU.subtract).then_inc(split_step, 1)
                nc.vector.tensor_copy(parts[BAND:2 * BAND], mid[BAND:2 * BAND, n])
                dve.wait_ge(split_step, step + 4)
                nc.vector.tensor_copy(parts[2 * BAND:3 * BAND], low[2 * BAND:3 * BAND, n]).then_inc(bias_split, 1)

            def copy_own(i, k, first, last):
                copy_weights(dve, nc.vector.tensor_copy, 1, i, k, first)
                if first and k < BANDS:
                    split_bias(k)

            def add_x(i, k, first, last):
                dve.wait_ge(multiplied, i * RING + k + 1)
                if last:
                    dve.wait_ge(early_stored, 16 * (GROUPS - OUTS))
                if last and k == RING - 1:
                    for t in range(TILES):
                        dve.wait_ge(multiplied, GROUPS + t)
                        nc.vector.tensor_tensor(result(i, k)[:, t], last_ps(t), x_sb[:, k, t], ALU.add).then_inc(added, 1)
                else:
                    nc.vector.tensor_tensor(result(i, k), out_ps[k][:], x_sb[:, k], ALU.add).then_inc(added, 1)

            passes(dve, (1, copy_own), (0, add_x))

        @block.tensor
        def _(pe):
            def gather_bias():
                pe.wait_ge(table_loaded, 16)
                for n in range(BANDS):
                    pe.wait_ge(has_category_made, n + 1)
                    if n == 1:
                        pe.wait_ge(first_made, 1)
                    nc.tensor.matmul(gather_ps[n], has_category[:, n].rearrange("c p b -> c (p b)"), table[:],
                                     start=True, stop=True).then_inc(bias_gathered, 1)

            def transpose_x(i, k, first, last):
                g = i * RING + k
                pe.wait_ge(x_loaded[k], 16 * (i + 1))
                if not (first and k < SLOTS):
                    pe.wait_ge(xt_ready, g - SLOTS + 1)
                for t in range(TILES):
                    for e in range(E):
                        last = nc.tensor.transpose(xt_ps[k % SLOTS][:, t, e, :], x_sb[:, k, t, e::E], ident[:])
                last.then_inc(transposed, 1)
                if first and k == 0:
                    gather_bias()

            def products(i, k, first, last):
                g = i * RING + k
                if not first:
                    pe.wait_ge(added, (i - 1) * RING + k + 1)
                pe.wait_ge(xt_ready, g + 1)

                def matrices(t, tile_ps, new_bank):
                    for half in range(2):
                        pe.wait_ge(w_copied[half], g * TILES + t + 1)
                    for e in range(E):
                        for b in range(PAIR):
                            nc.tensor.matmul(tile_ps[b * S:(b + 1) * S], xt_sb[:, k % SLOTS, t, e, b * S:(b + 1) * S],
                                             w_ring[:, k, t * PAIR + b, e, :],
                                             start=(new_bank and e == 0), stop=False, skip_group_check=True)

                def own_bias(t, tile_ps):
                    tile = g * TILES + t
                    band, at = tile // (BAND // PAIR), tile % (BAND // PAIR)
                    return nc.tensor.matmul(tile_ps, own_rows[:, bass.ds(at * PAIR, PAIR), :], bias_parts[:, band, :],
                                            start=False, stop=True, skip_group_check=True)

                if last and k == RING - 1:
                    for t in range(TILES):
                        matrices(t, last_ps(t), True)
                        own_bias(t, last_ps(t)).then_inc(multiplied, 1)
                    return
                for t in range(TILES):
                    matrices(t, out_ps[k][:, t, :], t == 0)
                if first and k == 0:
                    pe.wait_ge(own_rows_made, 1)
                    pe.wait_ge(bias_split, 1)
                if first and k == RING - 1:
                    pe.wait_ge(bias_split, BANDS)
                for t in range(TILES):
                    done = own_bias(t, out_ps[k][:, t, :])
                done.then_inc(multiplied, 1)

            pe.wait_ge(repeats_made, 1)
            nc.tensor.matmul(count_ps, ones_col[:], repeats[:], start=True, stop=True).then_inc(counted, 1)
            pe.wait_ge(ident_made, 1)

            passes(pe, (1, transpose_x), (0, products))


_INS = ["x", "itok_B_0_63", "L0_cond_W", "L0_cond_b"]


def kernel(**inputs):
    import numpy as np
    import concourse.bacc as bacc
    from concourse import mybir as mb
    from concourse.bass_utils import run_bass_kernel_spmd

    nc = bacc.Bacc("TRN2", target_bir_lowering=False, num_devices=1)
    arrays, args = {}, []
    for name in _INS:
        a = np.ascontiguousarray(inputs[name])
        arrays[f"in_{name}"] = a
        args.append(nc.dram_tensor(f"in_{name}", a.shape, mb.dt.from_np(a.dtype), kind="ExternalInput").ap())
    shape, dtype = inputs["x"].shape, np.dtype("float32")
    out = nc.dram_tensor("out", shape, mb.dt.from_np(dtype), kind="ExternalOutput").ap()
    conditional_residual(nc, *args, out)
    return run_bass_kernel_spmd(nc, [arrays], core_ids=[0]).results[0]["out"]
```
